# Optimizing a Trainium2 kernel written in Bass

```python
import numpy as np
import jax
import jax.numpy as jnp

def _softmax(x, axis=-1):
    return jax.nn.softmax(x, axis=axis)

def _gelu(x):
    return jax.nn.gelu(x, approximate=True)

def _silu(x):
    return jax.nn.silu(x)

def _sigmoid(x):
    return jax.nn.sigmoid(x)

def _layernorm(x, axis=-1, eps=1e-05):
    m = jnp.mean(x, axis=axis, keepdims=True)
    v = jnp.var(x, axis=axis, keepdims=True)
    return (x - m) / jnp.sqrt(v + eps)

def _scatter_add(tgt, idx, src, axis=0):
    return tgt.at[idx].add(src)

def _segment_sum(src, seg, n):
    return jax.ops.segment_sum(src, seg, n)
kernel_name = 'mk_rec_standalone_d1_rec_r8_548064'

def setup_inputs(seed: int=0):
    np.random.seed(seed)
    _w = jnp.asarray

    def _rec_inputs():
        import jax
        import jax.numpy as jnp
        _rk = jax.random.key(seed)
        r_dense = -0.00338568 + 1.0005 * jax.random.normal(jax.random.fold_in(_rk, 1), (2048, 13), jnp.float32)
        r_emb_indices = jnp.stack([jax.random.randint(jax.random.fold_in(jax.random.fold_in(_rk, 2), 0), (2048,), 6, 6250, jnp.int32), jax.random.randint(jax.random.fold_in(jax.random.fold_in(_rk, 2), 1), (2048,), 2, 49999, jnp.int32), jax.random.randint(jax.random.fold_in(jax.random.fold_in(_rk, 2), 2), (2048,), 5, 49995, jnp.int32), jax.random.randint(jax.random.fold_in(jax.random.fold_in(_rk, 2), 3), (2048,), 0, 49998, jnp.int32), jax.random.randint(jax.random.fold_in(jax.random.fold_in(_rk, 2), 4), (2048,), 2, 49999, jnp.int32), jax.random.randint(jax.random.fold_in(jax.random.fold_in(_rk, 2), 5), (2048,), 0, 49991, jnp.int32), jax.random.randint(jax.random.fold_in(jax.random.fold_in(_rk, 2), 6), (2048,), 0, 6250, jnp.int32), jax.random.randint(jax.random.fold_in(jax.random.fold_in(_rk, 2), 7), (2048,), 3, 6250, jnp.int32), jax.random.randint(jax.random.fold_in(jax.random.fold_in(_rk, 2), 8), (2048,), 0, 49997, jnp.int32), jax.random.randint(jax.random.fold_in(jax.random.fold_in(_rk, 2), 9), (2048,), 2, 49999, jnp.int32), jax.random.randint(jax.random.fold_in(jax.random.fold_in(_rk, 2), 10), (2048,), 1, 6250, jnp.int32), jax.random.randint(jax.random.fold_in(jax.random.fold_in(_rk, 2), 11), (2048,), 0, 49998, jnp.int32), jax.random.randint(jax.random.fold_in(jax.random.fold_in(_rk, 2), 12), (2048,), 0, 49996, jnp.int32), jax.random.randint(jax.random.fold_in(jax.random.fold_in(_rk, 2), 13), (2048,), 2, 6250, jnp.int32), jax.random.randint(jax.random.fold_in(jax.random.fold_in(_rk, 2), 14), (2048,), 2, 49998, jnp.int32), jax.random.randint(jax.random.fold_in(jax.random.fold_in(_rk, 2), 15), (2048,), 1, 49998, jnp.int32), jax.random.randint(jax.random.fold_in(jax.random.fold_in(_rk, 2), 16), (2048,), 4, 49991, jnp.int32), jax.random.randint(jax.random.fold_in(jax.random.fold_in(_rk, 2), 17), (2048,), 0, 49985, jnp.int32), jax.random.randint(jax.random.fold_in(jax.random.fold_in(_rk, 2), 18), (2048,), 3, 49997, jnp.int32), jax.random.randint(jax.random.fold_in(jax.random.fold_in(_rk, 2), 19), (2048,), 0, 49998, jnp.int32), jax.random.randint(jax.random.fold_in(jax.random.fold_in(_rk, 2), 20), (2048,), 3, 49997, jnp.int32), jax.random.randint(jax.random.fold_in(jax.random.fold_in(_rk, 2), 21), (2048,), 2, 49999, jnp.int32), jax.random.randint(jax.random.fold_in(jax.random.fold_in(_rk, 2), 22), (2048,), 6, 49998, jnp.int32), jax.random.randint(jax.random.fold_in(jax.random.fold_in(_rk, 2), 23), (2048,), 1, 49995, jnp.int32), jax.random.randint(jax.random.fold_in(jax.random.fold_in(_rk, 2), 24), (2048,), 4, 6250, jnp.int32), jax.random.randint(jax.random.fold_in(jax.random.fold_in(_rk, 2), 25), (2048,), 0, 49998, jnp.int32)], axis=0)
        return (r_dense, r_emb_indices)
    r_dense, r_emb_indices = _rec_inputs()

    def _L0_rec_setup():
        import jax, jax.numpy as jnp
        import numpy as np
        N_CAT, VOCAB, D = (26, 6250, 128)
        B, DENSE_NUM = (2048, 13)
        MLP = [512, 256, 128]
        PROJ = 512
        N = N_CAT + 1
        INTER = (N * N - N) // 2
        PROJ_IN = MLP[-1] + INTER
        key = jax.random.key(seed)
        ks = jax.random.split(key, 12)
        dense = jax.random.normal(ks[0], (B, DENSE_NUM), dtype=jnp.float32)
        emb_indices = jax.random.randint(ks[1], (N_CAT, B), 0, VOCAB, dtype=jnp.int64)

        def xav(k, fan_in, fan_out):
            std = np.sqrt(2.0 / (fan_in + fan_out)).astype(np.float32)
            return jax.random.normal(k, (fan_in, fan_out), dtype=jnp.float32) * std
        W0 = xav(ks[2], DENSE_NUM, MLP[0])
        b0 = jnp.zeros((MLP[0],), jnp.float32)
        W1 = xav(ks[3], MLP[0], MLP[1])
        b1 = jnp.zeros((MLP[1],), jnp.float32)
        W2 = xav(ks[4], MLP[1], MLP[2])
        b2 = jnp.zeros((MLP[2],), jnp.float32)
        emb_tables = jax.random.normal(ks[5], (N_CAT, VOCAB, D), dtype=jnp.float32) * 0.01
        Wp = xav(ks[6], PROJ_IN, PROJ)
        bp = jnp.zeros((PROJ,), jnp.float32)
        return {'dense': dense, 'emb_indices': emb_indices, 'W0': W0, 'b0': b0, 'W1': W1, 'b1': b1, 'W2': W2, 'b2': b2, 'emb_tables': emb_tables, 'Wp': Wp, 'bp': bp}
    _L0_rec_all = _L0_rec_setup()
    _L0_rec_in = {k: v for k, v in _L0_rec_all.items() if k in ('W0', 'b0', 'W1', 'b1', 'W2', 'b2', 'emb_tables', 'Wp', 'bp')}
    del _L0_rec_all
    return {'r_dense': r_dense, 'r_emb_indices': r_emb_indices, 'L0_rec_W0': _L0_rec_in['W0'], 'L0_rec_b0': _L0_rec_in['b0'], 'L0_rec_W1': _L0_rec_in['W1'], 'L0_rec_b1': _L0_rec_in['b1'], 'L0_rec_W2': _L0_rec_in['W2'], 'L0_rec_b2': _L0_rec_in['b2'], 'L0_rec_emb_tables': _L0_rec_in['emb_tables'], 'L0_rec_Wp': _L0_rec_in['Wp'], 'L0_rec_bp': _L0_rec_in['bp']}

def reference(r_dense, r_emb_indices, L0_rec_W0, L0_rec_b0, L0_rec_W1, L0_rec_b1, L0_rec_W2, L0_rec_b2, L0_rec_emb_tables, L0_rec_Wp, L0_rec_bp):
    import jax
    import jax.numpy as jnp

    def _L0_rec_ref(dense, emb_indices, W0, b0, W1, b1, W2, b2, emb_tables, Wp, bp):
        import jax, jax.numpy as jnp
        import numpy as np
        N_CAT, VOCAB, D = (26, 6250, 128)
        B, DENSE_NUM = (2048, 13)
        MLP = [512, 256, 128]
        PROJ = 512
        N = N_CAT + 1
        INTER = (N * N - N) // 2
        PROJ_IN = MLP[-1] + INTER
        h = jax.nn.relu(dense @ W0 + b0)
        h = jax.nn.relu(h @ W1 + b1)
        b_mlp_out = h @ W2 + b2
        emb = jax.vmap(lambda tbl, idx: tbl[idx])(emb_tables, emb_indices)
        sparse = jnp.transpose(emb, (1, 0, 2))
        T = jnp.concatenate([b_mlp_out[:, None, :], sparse], axis=1)
        Z = jnp.einsum('bnd,bmd->bnm', T, T)
        row, col = jnp.triu_indices(N, k=1)
        Z_flat = Z[:, row, col]
        combined = jnp.concatenate([b_mlp_out, Z_flat], axis=1)
        return combined @ Wp + bp
    y = _L0_rec_ref(r_dense, r_emb_indices, L0_rec_W0, L0_rec_b0, L0_rec_W1, L0_rec_b1, L0_rec_W2, L0_rec_b2, L0_rec_emb_tables, L0_rec_Wp, L0_rec_bp)
    return y

_drawn_inputs = setup_inputs


def setup_inputs(seed=0):
    import zlib

    import numpy as np

    out = dict(_drawn_inputs(seed))
    spreads = {'L0_rec_b0': (0.0, 0.1),
     'L0_rec_b1': (0.0, 0.1),
     'L0_rec_b2': (0.0, 0.1),
     'L0_rec_bp': (0.0, 0.1)}
    factors = {}
    for name, (base, spread) in spreads.items():
        noise = np.random.default_rng([zlib.crc32(name.encode()), seed]).standard_normal(out[name].shape)
        drawn = base * np.exp(spread * noise) if base else spread * noise
        out[name] = jnp.asarray(drawn.astype(out[name].dtype))
    for name, factor in factors.items():
        out[name] = (out[name] * factor).astype(out[name].dtype)
    return out
```

```python
import concourse.bass as bass
from concourse import mybir
from contextlib import ExitStack


def recommender_kernel(nc, dense, indices, w0, b0, w1, b1, w2, b2, tables, wp, bp, out):
    fp32 = mybir.dt.float32
    i32 = mybir.dt.int32
    ALU = mybir.AluOpType
    ACT = mybir.ActivationFunctionType

    P = 128
    Q = 32
    BATCH, FEATURES = dense.shape
    TABLES, VOCAB, D = tables.shape
    H0, H1, OUT = w0.shape[1], w1.shape[1], wp.shape[1]
    TILES = BATCH // P
    SLOTS = 2
    STEPS = TILES // SLOTS
    N = TABLES + 1
    HALF = (N - 1) // 2
    ROWS = 9
    CHUNKS = N // ROWS
    PAIRS = ROWS * HALF
    assert N % 2 == 1 and N % ROWS == 0 and PAIRS < P and D == P and w2.shape[1] == D
    GROUP = 4
    GROUPS = -(-TABLES // GROUP)
    K0, K1 = H0 // P, H1 // P
    MLP_MM = K0 + K1 + 1
    MLP_EV = K0 + K1 + SLOTS

    MLP_LOADS = 5 + K1

    table_rows = tables.rearrange("t v d -> (t v) d")
    out_rows = out.rearrange("(p t) n -> t p n", t=TILES)

    def group_tables(k):
        return range(k * GROUP, min(TABLES, (k + 1) * GROUP))

    ctx = ExitStack()
    with ctx:
        def sb(name, shape, dt=fp32):
            return ctx.enter_context(nc.sbuf_tensor(name, shape, dt))

        def ps(name, shape):
            return ctx.enter_context(nc.psum_tensor(name, shape, fp32))

        def sem(name):
            return ctx.enter_context(nc.semaphore(name))

        def slot_sems(name):
            return [sem(f"{name}{s}") for s in range(SLOTS)]

        ident = sb("ident", [P, P])
        raw_idx = sb("raw_idx", [P, TABLES, TILES], i32)
        clamped = sb("clamped", [P, TILES, TABLES])
        wrap = sb("wrap", [P, TILES, TABLES])
        base = sb("base", [P, TABLES], i32)
        row_idx = sb("row_idx", [P, TILES + SLOTS, TABLES], i32)
        idx = [sb(f"idx{s}", [P, TABLES], i32) for s in range(SLOTS)]
        dense_sb = sb("dense_sb", [P, TILES, FEATURES])
        denseT = sb("denseT", [FEATURES + 1, TILES * P])
        features = sb("features", [FEATURES + 1, SLOTS * P])
        w0_sb = sb("w0_sb", [FEATURES + 1, H0])
        w1_sb = sb("w1_sb", [P, K0, H1])
        w2_sb = sb("w2_sb", [P, K1, D])
        b1_sb = sb("b1_sb", [P, K1])
        b2_sb = sb("b2_sb", [P, 1])
        h0 = sb("h0", [P, K0, SLOTS * P])
        h1 = sb("h1", [P, K1, SLOTS * P])
        wp_mlp = sb("wp_mlp", [P, OUT])
        wp_pair = sb("wp_pair", [PAIRS + 1, CHUNKS, OUT])
        rows = [sb(f"rows{s}", [P, TABLES, D]) for s in range(SLOTS)]
        vecT = [sb(f"vecT{s}", [P, P, N]) for s in range(SLOTS)]
        prod = sb("prod", [P, N + HALF, Q])
        pairs = sb("pairs", [P, CHUNKS, PAIRS])
        pairT = sb("pairT", [P, CHUNKS, P])
        out_sb = [sb(f"out_sb{s}", [P, OUT]) for s in range(SLOTS)]

        trans_ps = [ps(f"trans_ps{k}", [P, GROUP, P]) for k in range(2)]
        gram_ps = ps("gram_ps", [P, 2, 512])
        pair_ps = ps("pair_ps", [P, CHUNKS + 1, P])
        out_ps = ps("out_ps", [P, OUT])
        mlp_ps = ps("mlp_ps", [P, 2, 512])

        idx_loaded = sem("idx_loaded")
        dense_loaded = sem("dense_loaded")
        mlp_loaded = sem("mlp_loaded")
        wp_loaded = sem("wp_loaded")
        ident_zeroed = sem("ident_zeroed")
        ident_ready = sem("ident_ready")
        base_ready = sem("base_ready")
        idx_step = sem("idx_step")
        ones_ready = sem("ones_ready")
        gram_zeroed = sem("gram_zeroed")
        denseT_done = sem("denseT_done")
        features_ready = sem("features_ready")
        denseT_copied = sem("denseT_copied")
        idx_ready = slot_sems("idx_ready")
        gather_begun = sem("gather_begun")
        gathered = [[sem(f"gathered{s}_{k}") for k in range(GROUPS)] for s in range(SLOTS)]
        transposed = sem("transposed")
        copied_dve = sem("copied_dve")
        copied_act = sem("copied_act")
        mlp_done = sem("mlp_done")
        mlp_copied = sem("mlp_copied")
        gram_done = sem("gram_done")
        turned = sem("turned")
        wrapped = sem("wrapped")
        packed = sem("packed")
        pairs_done = sem("pairs_done")
        pairs_copied = sem("pairs_copied")
        projected = sem("projected")
        out_copied = sem("out_copied")
        stored = slot_sems("stored")

        def wp_loads():
            def row(lo, hi):
                return D + lo * (N - 1) - lo * (lo - 1) // 2 + hi - lo - 1
            for r in range(N - 1):
                yield r // ROWS, HALF * (r % ROWS), 1, min(HALF, N - 1 - r), row(r, r + 1)
            for lo in range(N - HALF - 1):
                for c in range(CHUNKS):
                    first, last = max(lo + HALF + 1, ROWS * c), min(N, ROWS * (c + 1))
                    if first < last:
                        k = lo + N - first
                        yield c, HALF * (first - ROWS * c) + k - 1, HALF - 1, last - first, row(lo, first)

        WP_LOADS = list(wp_loads())
        assert sum(load[3] for load in WP_LOADS) == CHUNKS * PAIRS

        block = ctx.enter_context(nc.Block())

        @block.sync
        def _(sp):
            sp.dma_start(raw_idx[:, :, :], indices.rearrange("n (p t) -> p n t", t=TILES)).then_inc(idx_loaded, 16)
            sp.dma_start(wp_mlp[:, :], wp[0:D, :]).then_inc(wp_loaded, 16)
            sp.dma_start(wp_pair[PAIRS:PAIRS + 1, CHUNKS - 1, :], bp.rearrange("(a n) -> a n", a=1))\
                .then_inc(wp_loaded, 16)
            for chunk, part, step, count, first in WP_LOADS:
                sp.dma_start(wp_pair[part:part + step * (count - 1) + 1:step, chunk, :],
                             wp[first:first + count, :]).then_inc(wp_loaded, 16)
            with sp.Fori(0, STEPS) as i:
                for s in range(SLOTS):
                    sp.wait_ge(out_copied, SLOTS * i + s + 1)
                    sp.dma_start(out_rows[bass.ds(SLOTS * i + s, 1), :, :].rearrange("a p n -> (a p) n"),
                                 out_sb[s][:, :]).then_inc(stored[s], 16)
            for s in range(SLOTS):
                sp.wait_ge(stored[s], 16 * STEPS)

        @block.gpsimd
        def _(pool):
            pool.memset(ident[:, :], 0.0).then_inc(ident_zeroed, 1)
            pool.iota(base[:, :], [[VOCAB, TABLES]], base=0, channel_multiplier=0).then_inc(base_ready, 1)
            pool.wait_ge(ident_zeroed, 1)
            pool.affine_select(out=ident[:, :], in_=ident[:, :], compare_op=ALU.not_equal, fill=1.0, base=0,
                               pattern=[[-1, P]], channel_multiplier=1).then_inc(ident_ready, 1)
            with pool.Fori(0, STEPS) as i:
                for s in range(SLOTS):
                    pool.wait_ge(idx_ready[s], i + 1)
                    pool.sem_inc(gather_begun, 1)
                    for n in range(TABLES):
                        pool.indirect_dma_start(
                            out=rows[s][:, n, :], out_offset=None, in_=table_rows,
                            in_offset=bass.IndirectOffsetOnAxis(ap=idx[s][:, n:n + 1], axis=0),
                        ).then_inc(gathered[s][n // GROUP], 16)

        @block.tensor
        def _(pe):
            pe.wait_ge(ident_ready, 1)
            pe.wait_ge(dense_loaded, 16)
            for t in range(TILES):
                if t % 4 == 0 and t >= 8:
                    pe.wait_ge(denseT_copied, t // 4 - 1)
                mm = pe.matmul(mlp_ps[0:FEATURES, (t // 4) % 2, (t % 4) * P:(t % 4 + 1) * P],
                               dense_sb[:, t, :], ident[:, :], start=True, stop=True)
                if t % 4 == 3:
                    mm.then_inc(denseT_done, 1)
            pe.wait_ge(mlp_loaded, MLP_LOADS * 16)
            with pe.Fori(0, STEPS) as i:
                for c in range(MLP_MM):
                    pe.wait_ge(mlp_copied, MLP_EV * i + (c - 1 if c >= 2 else 0))
                    dst = mlp_ps[:, c % 2, 0:SLOTS * P]
                    if c < K0:
                        pe.wait_ge(features_ready, i + 1)
                        mm = pe.matmul(dst, w0_sb[:, c * P:(c + 1) * P], features[:, :], start=True, stop=True)
                    elif c < K0 + K1:
                        pe.wait_ge(mlp_copied, MLP_EV * i + K0)
                        for k in range(K0):
                            mm = pe.matmul(dst, w1_sb[:, k, (c - K0) * P:(c - K0 + 1) * P], h0[:, k, :],
                                           start=(k == 0), stop=(k == K0 - 1))
                    else:
                        pe.wait_ge(mlp_copied, MLP_EV * i + K0 + K1)
                        for k in range(K1):
                            mm = pe.matmul(dst, w2_sb[:, k, :], h1[:, k, :], start=(k == 0), stop=(k == K1 - 1))
                    mm.then_inc(mlp_done, 1)
                for s in range(SLOTS):
                    for k in range(GROUPS):
                        g = GROUPS * s + k
                        pe.wait_ge(gathered[s][k], 16 * len(group_tables(k)) * (i + 1))
                        pe.wait_ge((copied_dve, copied_act)[g % 2], GROUPS * i + g // 2)
                        for n in group_tables(k):
                            mm = pe.transpose(trans_ps[g % 2][:, n % GROUP, :], rows[s][:, n, :], ident[:, :])
                        mm.then_inc(transposed, 1)
                    pe.wait_ge(copied_dve, GROUPS * i + (GROUPS * (s + 1) + 1) // 2)
                    pe.wait_ge(copied_act, GROUPS * i + GROUPS * (s + 1) // 2)
                    pe.wait_ge(mlp_copied, MLP_EV * i + K0 + K1 + s + 1)
                    pe.wait_ge(turned, SLOTS * i + s)
                    if s == 0:
                        pe.wait_ge(gram_zeroed, 1)
                    for g in range(Q):
                        for j in range(P // Q):
                            v = vecT[s][:, Q * j + g, :]
                            mm = pe.matmul(gram_ps[Q * j:Q * j + N, g // 16, (g % 16) * N:(g % 16 + 1) * N],
                                           v, v, start=True, stop=True)
                    mm.then_inc(gram_done, 1)
                    pe.wait_ge(packed, SLOTS * i + s + 1)
                    pe.wait_ge(pairs_copied, SLOTS * i + s)
                    for c in range(CHUNKS):
                        mm = pe.transpose(pair_ps[0:PAIRS, c, :], pairs[:, c, :], ident[:, :])
                    mm.then_inc(pairs_done, 1)
                    pe.wait_ge(out_copied, SLOTS * i + s)
                    if s == 0:
                        pe.wait_ge(wp_loaded, 16 * (2 + len(WP_LOADS)))
                        pe.wait_ge(ones_ready, 2)
                    pe.matmul(out_ps[:, :], vecT[s][:, :, 0], wp_mlp[:, :], start=True, stop=False)
                    pe.wait_ge(pairs_copied, SLOTS * i + s + 1)
                    for c in range(CHUNKS):
                        k = PAIRS + (c == CHUNKS - 1)
                        mm = pe.matmul(out_ps[:, :], pairT[0:k, c, :], wp_pair[0:k, c, :],
                                       start=False, stop=(c == CHUNKS - 1))
                    mm.then_inc(projected, 1)

        @block.scalar
        def _(act):
            act.dma_start(dense_sb[:, :, :], dense.rearrange("(p t) f -> p t f", t=TILES)).then_inc(dense_loaded, 16)
            act.dma_start(w0_sb[0:FEATURES, :], w0).then_inc(mlp_loaded, 16)
            act.dma_start(w0_sb[FEATURES:FEATURES + 1, :], b0.rearrange("(a n) -> a n", a=1)).then_inc(mlp_loaded, 16)
            act.dma_start(w1_sb[:, :, :], w1.rearrange("(k p) n -> p k n", p=P)).then_inc(mlp_loaded, 16)
            act.dma_start(w2_sb[:, :, :], w2.rearrange("(k p) n -> p k n", p=P)).then_inc(mlp_loaded, 16)
            for k in range(K1):
                act.dma_start(b1_sb[:, k:k + 1], b1[k * P:(k + 1) * P].rearrange("(p a) -> p a", a=1))\
                    .then_inc(mlp_loaded, 16)
            act.dma_start(b2_sb[:, :], b2.rearrange("(p a) -> p a", a=1)).then_inc(mlp_loaded, 16)
            act.wait_ge(ones_ready, 1)
            for h in range(TILES // 4):
                act.wait_ge(denseT_done, h + 1)
                act.activation(denseT[0:FEATURES, h * 4 * P:(h + 1) * 4 * P], mlp_ps[0:FEATURES, h % 2, :],
                               ACT.Copy).then_inc(denseT_copied, 1)
            act.wait_ge(mlp_loaded, MLP_LOADS * 16)
            with act.Fori(0, STEPS) as i:
                act.wait_ge(denseT_copied, TILES // 4)
                act.activation(features[:, :], denseT[:, bass.ds(i * (SLOTS * P), SLOTS * P)], ACT.Copy)\
                    .then_inc(features_ready, 1)
                for c in range(MLP_MM):
                    act.wait_ge(mlp_done, MLP_MM * i + c + 1)
                    src = mlp_ps[:, c % 2, 0:SLOTS * P]
                    if c < K0:
                        act.activation(h0[:, c, :], src, ACT.Relu).then_inc(mlp_copied, 1)
                    elif c < K0 + K1:
                        k = c - K0
                        act.activation(h1[:, k, :], src, ACT.Relu, bias=b1_sb[:, k:k + 1]).then_inc(mlp_copied, 1)
                    else:
                        for s in range(SLOTS):
                            act.activation(vecT[s][:, :, 0], src[:, s * P:(s + 1) * P], ACT.Identity,
                                           bias=b2_sb[:, 0:1]).then_inc(mlp_copied, 1)
                for s in range(SLOTS):
                    for k in range(GROUPS):
                        g = GROUPS * s + k
                        if g % 2:
                            act.wait_ge(transposed, SLOTS * GROUPS * i + g + 1)
                            m = len(group_tables(k))
                            act.activation(vecT[s][:, :, 1 + GROUP * k:1 + GROUP * k + m].rearrange("d b n -> d n b"),
                                           trans_ps[1][:, 0:m, :], ACT.Copy).then_inc(copied_act, 1)
                    act.wait_ge(turned, SLOTS * i + s + 1)
                    act.activation(prod[:, N:N + HALF, N - HALF:N], prod[:, 0:HALF, N - HALF:N], ACT.Copy)\
                        .then_inc(wrapped, 1)
                    act.wait_ge(wrapped, SLOTS * i + s + 1)
                    first = prod[:, 1, 0:1]
                    src = bass.AP(tensor=first.tensor, offset=first.offset,
                                  ap=[list(first.ap[0]), [Q + 1, N], [Q, HALF]])
                    act.activation(pairs[:, :, :].rearrange("p c (r k) -> p (c r) k", k=HALF), src, ACT.Copy)\
                        .then_inc(packed, 1)
                    act.wait_ge(projected, SLOTS * i + s + 1)
                    act.wait_ge(stored[s], 16 * i)
                    act.activation(out_sb[s][:, :], out_ps[:, :], ACT.Copy).then_inc(out_copied, 1)

        @block.vector
        def _(dve):
            dve.memset(denseT[:, :], 1.0).then_inc(ones_ready, 1)
            dve.memset(pairT[:, :, :], 1.0).then_inc(ones_ready, 1)
            dve.memset(gram_ps[:, :, :], 0.0).then_inc(gram_zeroed, 1)
            dve.memset(row_idx[:, TILES:TILES + SLOTS, :], 0).then_inc(idx_step, 1)
            dve.wait_ge(idx_loaded, 16)
            dve.tensor_scalar(clamped[:, :, :], raw_idx[:, :, :].rearrange("p n t -> p t n"),
                              float(VOCAB - 1), float(-VOCAB), ALU.min, ALU.max).then_inc(idx_step, 1)
            dve.wait_ge(idx_step, 2)
            dve.tensor_scalar(wrap[:, :, :], clamped[:, :, :], 0.0, float(VOCAB), ALU.is_lt, ALU.mult)\
                .then_inc(idx_step, 1)
            dve.wait_ge(idx_step, 3)
            dve.tensor_tensor(clamped[:, :, :], clamped[:, :, :], wrap[:, :, :], ALU.add).then_inc(idx_step, 1)
            dve.wait_ge(idx_step, 4)
            dve.wait_ge(base_ready, 1)
            dve.tensor_tensor(row_idx[:, 0:TILES, :], clamped[:, :, :],
                              base[:, :].unsqueeze(1).to_broadcast([P, TILES, TABLES]), ALU.add)\
                .then_inc(idx_step, 1)
            dve.wait_ge(idx_step, 5)
            for s in range(SLOTS):
                dve.tensor_copy(idx[s][:, :], row_idx[:, s, :]).then_inc(idx_ready[s], 1)
            with dve.Fori(0, STEPS) as i:
                for s in range(SLOTS):
                    for k in range(GROUPS):
                        g = GROUPS * s + k
                        if g % 2 == 0:
                            dve.wait_ge(transposed, SLOTS * GROUPS * i + g + 1)
                            m = len(group_tables(k))
                            dve.tensor_copy(vecT[s][:, :, 1 + GROUP * k:1 + GROUP * k + m].rearrange("d b n -> d n b"),
                                            trans_ps[0][:, 0:m, :]).then_inc(copied_dve, 1)
                    dve.wait_ge(transposed, SLOTS * GROUPS * i + GROUPS * (s + 1))
                    dve.tensor_copy(idx[s][:, :],
                                    row_idx[:, bass.ds(SLOTS * i + SLOTS + s, 1), :].rearrange("p a n -> p (a n)"))\
                        .then_inc(idx_ready[s], 1)
                    dve.wait_ge(gram_done, SLOTS * i + s + 1)
                    src = bass.AP(tensor=gram_ps[:, :, :].tensor, offset=gram_ps[:, :, :].offset,
                                  ap=[list(gram_ps[:, :, :].ap[0]), [1, N], [512, 2], [N, 16]])
                    dve.transpose(prod[:, 0:N, :], src).then_inc(turned, 1)
                    dve.wait_ge(pairs_done, SLOTS * i + s + 1)
                    dve.tensor_copy(pairT[0:PAIRS, :, :], pair_ps[0:PAIRS, 0:CHUNKS, :]).then_inc(pairs_copied, 1)


_INS = ['r_dense', 'r_emb_indices', 'L0_rec_W0', 'L0_rec_b0', 'L0_rec_W1', 'L0_rec_b1', 'L0_rec_W2',
        'L0_rec_b2', 'L0_rec_emb_tables', 'L0_rec_Wp', 'L0_rec_bp']
_OUTS = [((2048, 512), 'float32')]


def kernel(**inputs):
    import numpy as _np
    import concourse.bacc as _bacc
    from concourse import mybir as _mybir
    from concourse.bass_utils import run_bass_kernel_spmd as _run

    nc = _bacc.Bacc("TRN2", target_bir_lowering=False, num_devices=1)
    arrays, args = {}, []
    for name in _INS:
        a = _np.ascontiguousarray(inputs[name])
        arrays[f"in_{name}_dram"] = a
        args.append(nc.dram_tensor(f"in_{name}_dram", a.shape, _mybir.dt.from_np(a.dtype), kind="ExternalInput").ap())
    for i, (shape, dtype) in enumerate(_OUTS):
        dt = _mybir.dt.from_np(_np.dtype(dtype))
        args.append(nc.dram_tensor(f"out_{i}_dram", shape, dt, kind="ExternalOutput").ap())
    recommender_kernel(nc, *args)
    r = _run(nc, [arrays], core_ids=[0])
    got = tuple(r.results[0][f"out_{i}_dram"] for i in range(len(_OUTS)))
    return got[0]
```

```python
import concourse.bass as bass
from concourse import mybir
from contextlib import ExitStack


def recommender_kernel(nc, dense, indices, w0, b0, w1, b1, w2, b2, tables, wp, bp, out):
    fp32 = mybir.dt.float32
    i32 = mybir.dt.int32
    ALU = mybir.AluOpType
    ACT = mybir.ActivationFunctionType

    P = 128
    Q = 32
    BATCH, FEATURES = dense.shape
    TABLES, VOCAB, D = tables.shape
    H0, H1, OUT = w0.shape[1], w1.shape[1], wp.shape[1]
    TILES = BATCH // P
    SLOTS = 2
    STEPS = TILES // SLOTS
    N = TABLES + 1
    HALF = (N - 1) // 2
    ROWS = 9
    CHUNKS = N // ROWS
    PAIRS = ROWS * HALF
    assert N % 2 == 1 and N % ROWS == 0 and PAIRS < P and D == P and w2.shape[1] == D
    GROUP = 4
    GROUPS = -(-TABLES // GROUP)
    K0, K1 = H0 // P, H1 // P
    MLP_MM = K0 + K1 + 1
    assert GROUPS == MLP_MM
    MLP_EV = K0 + K1 + SLOTS

    MLP_LOADS = 5 + K1

    table_rows = tables.rearrange("t v d -> (t v) d")
    out_rows = out.rearrange("(p t) n -> t p n", t=TILES)

    def group_tables(k):
        return range(k * GROUP, min(TABLES, (k + 1) * GROUP))

    ctx = ExitStack()
    with ctx:
        def sb(name, shape, dt=fp32):
            return ctx.enter_context(nc.sbuf_tensor(name, shape, dt))

        def ps(name, shape):
            return ctx.enter_context(nc.psum_tensor(name, shape, fp32))

        def sem(name):
            return ctx.enter_context(nc.semaphore(name))

        def slot_sems(name):
            return [sem(f"{name}{s}") for s in range(SLOTS)]

        ident = sb("ident", [P, P])
        raw_idx = sb("raw_idx", [TABLES, P, TILES], i32)
        clamped = sb("clamped", [TABLES, TILES, P])
        negative = sb("negative", [TABLES, TILES, P])
        base_i = sb("base_i", [TABLES, 1], i32)
        base = sb("base", [TABLES, 1])
        row_idx = sb("row_idx", [P, TILES + SLOTS, TABLES], i32)
        idx = [sb(f"idx{s}", [P, TABLES], i32) for s in range(SLOTS)]
        dense_sb = sb("dense_sb", [P, TILES, FEATURES])
        denseT = sb("denseT", [FEATURES + 1, TILES * P])
        features = sb("features", [FEATURES + 1, SLOTS * P])
        w0_sb = sb("w0_sb", [FEATURES + 1, H0])
        w1_sb = sb("w1_sb", [P, K0, H1])
        w2_sb = sb("w2_sb", [P, K1, D])
        b1_sb = sb("b1_sb", [P, K1])
        b2_sb = sb("b2_sb", [P, 1])
        h0 = sb("h0", [P, K0, SLOTS * P])
        h1 = sb("h1", [P, K1, SLOTS * P])
        wp_mlp = sb("wp_mlp", [P, OUT])
        wp_pair = sb("wp_pair", [PAIRS + 1, CHUNKS, OUT])
        rows = [sb(f"rows{s}", [P, TABLES, D]) for s in range(SLOTS)]
        vecT = [sb(f"vecT{s}", [P, P, N]) for s in range(SLOTS)]
        prod = sb("prod", [P, N + HALF, Q])
        pairs = sb("pairs", [P, CHUNKS, PAIRS])
        pairT = sb("pairT", [P, CHUNKS, P])
        out_sb = [sb(f"out_sb{s}", [P, OUT]) for s in range(SLOTS)]

        trans_ps = [ps(f"trans_ps{k}", [P, GROUP, P]) for k in range(2)]
        gram_ps = ps("gram_ps", [P, 2, 512])
        pair_ps = ps("pair_ps", [P, CHUNKS + 1, P])
        out_ps = ps("out_ps", [P, OUT])
        mlp_ps = ps("mlp_ps", [P, 2, 512])

        idx_loaded = sem("idx_loaded")
        dense_loaded = sem("dense_loaded")
        mlp_loaded = sem("mlp_loaded")
        wp_loaded = sem("wp_loaded")
        ident_zeroed = sem("ident_zeroed")
        ident_ready = sem("ident_ready")
        base_i_ready = sem("base_i_ready")
        rows_known = sem("rows_known")
        rows_turned = sem("rows_turned")
        out_sb_free = sem("out_sb_free")
        idx_step = sem("idx_step")
        ones_ready = sem("ones_ready")
        gram_zeroed = sem("gram_zeroed")
        denseT_done = sem("denseT_done")
        features_ready = sem("features_ready")
        denseT_copied = sem("denseT_copied")
        idx_ready = slot_sems("idx_ready")
        gather_begun = sem("gather_begun")
        gathered = [[sem(f"gathered{s}_{k}") for k in range(GROUPS)] for s in range(SLOTS)]
        transposed = sem("transposed")
        copied_dve = sem("copied_dve")
        copied_act = sem("copied_act")
        mlp_done = sem("mlp_done")
        mlp_copied = sem("mlp_copied")
        gram_done = sem("gram_done")
        turned = sem("turned")
        wrapped = sem("wrapped")
        packed = sem("packed")
        pairs_done = sem("pairs_done")
        pairs_copied = sem("pairs_copied")
        projected = sem("projected")
        out_copied = sem("out_copied")
        stored = slot_sems("stored")

        def wp_loads():
            def row(lo, hi):
                return D + lo * (N - 1) - lo * (lo - 1) // 2 + hi - lo - 1
            for r in range(N - 1):
                yield r // ROWS, HALF * (r % ROWS), 1, min(HALF, N - 1 - r), row(r, r + 1)
            for lo in range(N - HALF - 1):
                for c in range(CHUNKS):
                    first, last = max(lo + HALF + 1, ROWS * c), min(N, ROWS * (c + 1))
                    if first < last:
                        k = lo + N - first
                        yield c, HALF * (first - ROWS * c) + k - 1, HALF - 1, last - first, row(lo, first)

        WP_LOADS = list(wp_loads())
        assert sum(load[3] for load in WP_LOADS) == CHUNKS * PAIRS

        block = ctx.enter_context(nc.Block())

        @block.sync
        def _(sp):
            sp.dma_start(raw_idx[:, :, :], indices.rearrange("n (p t) -> n p t", t=TILES)).then_inc(idx_loaded, 16)
            sp.dma_start(wp_mlp[:, :], wp[0:D, :]).then_inc(wp_loaded, 16)
            sp.dma_start(wp_pair[PAIRS:PAIRS + 1, CHUNKS - 1, :], bp.rearrange("(a n) -> a n", a=1))\
                .then_inc(wp_loaded, 16)
            for chunk, part, step, count, first in WP_LOADS:
                sp.dma_start(wp_pair[part:part + step * (count - 1) + 1:step, chunk, :],
                             wp[first:first + count, :]).then_inc(wp_loaded, 16)
            with sp.Fori(0, STEPS) as i:
                for s in range(SLOTS):
                    sp.wait_ge(out_copied, SLOTS * i + s + 2)
                    sp.dma_start(out_rows[bass.ds(SLOTS * i + s, 1), :, :].rearrange("a p n -> (a p) n"),
                                 out_sb[s][:, :]).then_inc(stored[s], 16)
                    sp.wait_ge(stored[s], 16 * (i + 1))
                    sp.sem_inc(out_sb_free, 1)

        @block.gpsimd
        def _(pool):
            pool.memset(ident[:, :], 0.0).then_inc(ident_zeroed, 1)
            pool.iota(base_i[:, :], [[0, 1]], base=0, channel_multiplier=VOCAB).then_inc(base_i_ready, 1)
            pool.wait_ge(ident_zeroed, 1)
            pool.affine_select(out=ident[:, :], in_=ident[:, :], compare_op=ALU.not_equal, fill=1.0, base=0,
                               pattern=[[-1, P]], channel_multiplier=1).then_inc(ident_ready, 1)
            with pool.Fori(0, STEPS) as i:
                for s in range(SLOTS):
                    pool.wait_ge(idx_ready[s], i + 1)
                    pool.sem_inc(gather_begun, 1)
                    for n in range(TABLES):
                        pool.indirect_dma_start(
                            out=rows[s][:, n, :], out_offset=None, in_=table_rows,
                            in_offset=bass.IndirectOffsetOnAxis(ap=idx[s][:, n:n + 1], axis=0),
                        ).then_inc(gathered[s][n // GROUP], 16)

        @block.tensor
        def _(pe):
            pe.wait_ge(ident_ready, 1)
            pe.wait_ge(rows_known, 1)
            pe.transpose(trans_ps[0][:, 0, 0:TABLES], clamped[:, 0, :], ident[0:TABLES, 0:TABLES])\
                .then_inc(rows_turned, 1)
            pe.wait_ge(rows_known, 2)
            for t in range(1, TILES):
                mm = pe.transpose(out_ps[:, t * TABLES:(t + 1) * TABLES], clamped[:, t, :],
                                  ident[0:TABLES, 0:TABLES])
            mm.then_inc(rows_turned, 1)
            pe.wait_ge(dense_loaded, 16)
            for t in range(TILES):
                if t % 4 == 0 and t >= 8:
                    pe.wait_ge(denseT_copied, t // 4 - 1)
                mm = pe.matmul(mlp_ps[0:FEATURES, (t // 4) % 2, (t % 4) * P:(t % 4 + 1) * P],
                               dense_sb[:, t, :], ident[:, :], start=True, stop=True)
                if t % 4 == 3:
                    mm.then_inc(denseT_done, 1)
            pe.wait_ge(mlp_loaded, MLP_LOADS * 16)

            def mlp_block(i, c):
                pe.wait_ge(mlp_copied, MLP_EV * i + max(c, 1))
                dst = mlp_ps[:, c % 2, 0:SLOTS * P]
                if c < K0:
                    pe.wait_ge(features_ready, i + 1)
                    mm = pe.matmul(dst, w0_sb[:, c * P:(c + 1) * P], features[:, :], start=True, stop=True)
                elif c < K0 + K1:
                    pe.wait_ge(mlp_copied, MLP_EV * i + K0 + 1)
                    for k in range(K0):
                        mm = pe.matmul(dst, w1_sb[:, k, (c - K0) * P:(c - K0 + 1) * P], h0[:, k, :],
                                       start=(k == 0), stop=(k == K0 - 1))
                else:
                    pe.wait_ge(mlp_copied, MLP_EV * i + K0 + K1 + 1)
                    for k in range(K1):
                        mm = pe.matmul(dst, w2_sb[:, k, :], h1[:, k, :], start=(k == 0), stop=(k == K1 - 1))
                mm.then_inc(mlp_done, 1)

            with pe.Fori(0, STEPS) as i:
                pe.wait_ge(wp_loaded, 16 * (2 + len(WP_LOADS)))
                pe.wait_ge(ones_ready, 2)
                pe.wait_ge(gram_zeroed, 1)
                for s in range(SLOTS):
                    for k in range(GROUPS):
                        g = GROUPS * s + k
                        if s == 0:
                            mlp_block(i, k)
                        if k == GROUPS - 1:
                            pe.wait_ge((copied_dve, copied_act)[(g - 1) % 2], GROUPS * i + (g - 1) // 2 + 2)
                        pe.wait_ge(gathered[s][k], 16 * len(group_tables(k)) * (i + 1))
                        pe.wait_ge((copied_dve, copied_act)[g % 2], GROUPS * i + g // 2 + 1)
                        for n in group_tables(k):
                            mm = pe.transpose(trans_ps[g % 2][:, n % GROUP, :], rows[s][:, n, :], ident[:, :])
                        mm.then_inc(transposed, 1)
                    pe.wait_ge(mlp_copied, MLP_EV * i + K0 + K1 + s + 2)
                    pe.wait_ge((copied_dve, copied_act)[g % 2], GROUPS * i + g // 2 + 2)
                    for g in range(Q):
                        for j in range(P // Q):
                            v = vecT[s][:, Q * j + g, :]
                            mm = pe.matmul(gram_ps[Q * j:Q * j + N, g // 16, (g % 16) * N:(g % 16 + 1) * N],
                                           v, v, start=True, stop=True)
                    mm.then_inc(gram_done, 1)
                    pe.wait_ge(out_copied, SLOTS * i + s + 1)
                    pe.matmul(out_ps[:, :], vecT[s][:, :, 0], wp_mlp[:, :], start=True, stop=False)
                    pe.wait_ge(packed, SLOTS * i + s + 1)
                    for c in range(CHUNKS):
                        mm = pe.transpose(pair_ps[0:PAIRS, c, :], pairs[:, c, :], ident[:, :])
                    mm.then_inc(pairs_done, 1)
                    pe.wait_ge(pairs_copied, SLOTS * i + s + 2)
                    for c in range(CHUNKS):
                        k = PAIRS + (c == CHUNKS - 1)
                        mm = pe.matmul(out_ps[:, :], pairT[0:k, c, :], wp_pair[0:k, c, :],
                                       start=False, stop=(c == CHUNKS - 1))
                    mm.then_inc(projected, 1)

        @block.scalar
        def _(act):
            act.dma_start(dense_sb[:, :, :], dense.rearrange("(p t) f -> p t f", t=TILES)).then_inc(dense_loaded, 16)
            act.dma_start(w0_sb[0:FEATURES, :], w0).then_inc(mlp_loaded, 16)
            act.dma_start(w0_sb[FEATURES:FEATURES + 1, :], b0.rearrange("(a n) -> a n", a=1)).then_inc(mlp_loaded, 16)
            act.dma_start(w1_sb[:, :, :], w1.rearrange("(k p) n -> p k n", p=P)).then_inc(mlp_loaded, 16)
            act.dma_start(w2_sb[:, :, :], w2.rearrange("(k p) n -> p k n", p=P)).then_inc(mlp_loaded, 16)
            for k in range(K1):
                act.dma_start(b1_sb[:, k:k + 1], b1[k * P:(k + 1) * P].rearrange("(p a) -> p a", a=1))\
                    .then_inc(mlp_loaded, 16)
            act.dma_start(b2_sb[:, :], b2.rearrange("(p a) -> p a", a=1)).then_inc(mlp_loaded, 16)
            for first in (mlp_copied, copied_act, out_copied):
                act.sem_inc(first, 1)
            act.sem_inc(out_sb_free, SLOTS)
            act.wait_ge(ones_ready, 1)
            for h in range(TILES // 4):
                act.wait_ge(denseT_done, h + 1)
                act.activation(denseT[0:FEATURES, h * 4 * P:(h + 1) * 4 * P], mlp_ps[0:FEATURES, h % 2, :],
                               ACT.Copy).then_inc(denseT_copied, 1)
            act.wait_ge(mlp_loaded, MLP_LOADS * 16)

            def mlp_copy(i, c):
                act.wait_ge(mlp_done, MLP_MM * i + c + 1)
                src = mlp_ps[:, c % 2, 0:SLOTS * P]
                if c < K0:
                    act.activation(h0[:, c, :], src, ACT.Relu).then_inc(mlp_copied, 1)
                elif c < K0 + K1:
                    k = c - K0
                    act.activation(h1[:, k, :], src, ACT.Relu, bias=b1_sb[:, k:k + 1]).then_inc(mlp_copied, 1)
                else:
                    for s in range(SLOTS):
                        act.activation(vecT[s][:, :, 0], src[:, s * P:(s + 1) * P], ACT.Identity,
                                       bias=b2_sb[:, 0:1]).then_inc(mlp_copied, 1)

            with act.Fori(0, STEPS) as i:
                act.wait_ge(denseT_copied, TILES // 4)
                act.activation(features[:, :], denseT[:, bass.ds(i * (SLOTS * P), SLOTS * P)], ACT.Copy)\
                    .then_inc(features_ready, 1)
                for s in range(SLOTS):
                    for k in range(GROUPS):
                        g = GROUPS * s + k
                        if s == 0:
                            mlp_copy(i, k)
                        if g % 2:
                            act.wait_ge(transposed, SLOTS * GROUPS * i + g + 1)
                            m = len(group_tables(k))
                            act.activation(vecT[s][:, :, 1 + GROUP * k:1 + GROUP * k + m].rearrange("d b n -> d n b"),
                                           trans_ps[1][:, 0:m, :], ACT.Copy).then_inc(copied_act, 1)
                    act.wait_ge(turned, SLOTS * i + s + 2)
                    act.activation(prod[:, N:N + HALF, N - HALF:N], prod[:, 0:HALF, N - HALF:N], ACT.Copy)\
                        .then_inc(wrapped, 1)
                    act.wait_ge(wrapped, SLOTS * i + s + 1)
                    first = prod[:, 1, 0:1]
                    src = bass.AP(tensor=first.tensor, offset=first.offset,
                                  ap=[list(first.ap[0]), [Q + 1, N], [Q, HALF]])
                    act.activation(pairs[:, :, :].rearrange("p c (r k) -> p (c r) k", k=HALF), src, ACT.Copy)\
                        .then_inc(packed, 1)
                    act.wait_ge(projected, SLOTS * i + s + 1)
                    act.wait_ge(out_sb_free, SLOTS * i + s + 1)
                    act.activation(out_sb[s][:, :], out_ps[:, :], ACT.Copy).then_inc(out_copied, 1)

        @block.vector
        def _(dve):
            for first in (copied_dve, turned, pairs_copied):
                dve.sem_inc(first, 1)
            dve.wait_ge(base_i_ready, 1)
            dve.tensor_copy(base[:, :], base_i[:, :]).then_inc(idx_step, 1)
            dve.wait_ge(idx_loaded, 16)
            done = 1
            for first, last in ((0, 1), (1, TILES)):
                part = clamped[:, first:last, :]
                below = negative[:, first:last, :]
                dve.tensor_scalar(part, raw_idx[:, :, first:last].rearrange("n p t -> n t p"),
                                  float(VOCAB - 1), float(-VOCAB), ALU.min, ALU.max).then_inc(idx_step, 1)
                done += 1
                dve.wait_ge(idx_step, done)
                dve.tensor_scalar(below, part, 0.0, float(VOCAB), ALU.is_lt, ALU.mult).then_inc(idx_step, 1)
                done += 1
                dve.wait_ge(idx_step, done)
                dve.scalar_tensor_tensor(out=part, in0=part, scalar=base[:, 0:1], in1=below,
                                         op0=ALU.add, op1=ALU.add).then_inc(rows_known, 1)
                if first == 0:
                    dve.wait_ge(rows_turned, 1)
                    dve.tensor_copy(idx[0][:, :], trans_ps[0][:, 0, 0:TABLES]).then_inc(idx_ready[0], 1)
            dve.memset(denseT[:, :], 1.0).then_inc(ones_ready, 1)
            dve.memset(row_idx[:, TILES:TILES + SLOTS, :], 0).then_inc(idx_step, 1)
            dve.wait_ge(rows_turned, 2)
            dve.tensor_copy(row_idx[:, 1:TILES, :],
                            out_ps[:, TABLES:TILES * TABLES].rearrange("p (t n) -> p t n", n=TABLES))\
                .then_inc(idx_step, 1)
            dve.wait_ge(idx_step, done + 2)
            for s in range(1, SLOTS):
                dve.tensor_copy(idx[s][:, :], row_idx[:, s, :]).then_inc(idx_ready[s], 1)
            dve.memset(pairT[:, :, :], 1.0).then_inc(ones_ready, 1)
            dve.memset(gram_ps[:, :, :], 0.0).then_inc(gram_zeroed, 1)
            with dve.Fori(0, STEPS) as i:
                for s in range(SLOTS):
                    for k in range(GROUPS):
                        g = GROUPS * s + k
                        if g % 2 == 0:
                            dve.wait_ge(transposed, SLOTS * GROUPS * i + g + 1)
                            m = len(group_tables(k))
                            dve.tensor_copy(vecT[s][:, :, 1 + GROUP * k:1 + GROUP * k + m].rearrange("d b n -> d n b"),
                                            trans_ps[0][:, 0:m, :]).then_inc(copied_dve, 1)
                    dve.wait_ge(transposed, SLOTS * GROUPS * i + GROUPS * (s + 1))
                    dve.tensor_copy(idx[s][:, :],
                                    row_idx[:, bass.ds(SLOTS * i + SLOTS + s, 1), :].rearrange("p a n -> p (a n)"))\
                        .then_inc(idx_ready[s], 1)
                    dve.wait_ge(gram_done, SLOTS * i + s + 1)
                    src = bass.AP(tensor=gram_ps[:, :, :].tensor, offset=gram_ps[:, :, :].offset,
                                  ap=[list(gram_ps[:, :, :].ap[0]), [1, N], [512, 2], [N, 16]])
                    dve.transpose(prod[:, 0:N, :], src).then_inc(turned, 1)
                    dve.wait_ge(pairs_done, SLOTS * i + s + 1)
                    dve.tensor_copy(pairT[0:PAIRS, :, :], pair_ps[0:PAIRS, 0:CHUNKS, :]).then_inc(pairs_copied, 1)


_INS = ['r_dense', 'r_emb_indices', 'L0_rec_W0', 'L0_rec_b0', 'L0_rec_W1', 'L0_rec_b1', 'L0_rec_W2',
        'L0_rec_b2', 'L0_rec_emb_tables', 'L0_rec_Wp', 'L0_rec_bp']
_OUTS = [((2048, 512), 'float32')]


def kernel(**inputs):
    import numpy as _np
    import concourse.bacc as _bacc
    from concourse import mybir as _mybir
    from concourse.bass_utils import run_bass_kernel_spmd as _run

    nc = _bacc.Bacc("TRN2", target_bir_lowering=False, num_devices=1)
    arrays, args = {}, []
    for name in _INS:
        a = _np.ascontiguousarray(inputs[name])
        arrays[f"in_{name}_dram"] = a
        args.append(nc.dram_tensor(f"in_{name}_dram", a.shape, _mybir.dt.from_np(a.dtype), kind="ExternalInput").ap())
    for i, (shape, dtype) in enumerate(_OUTS):
        dt = _mybir.dt.from_np(_np.dtype(dtype))
        args.append(nc.dram_tensor(f"out_{i}_dram", shape, dt, kind="ExternalOutput").ap())
    recommender_kernel(nc, *args)
    r = _run(nc, [arrays], core_ids=[0])
    got = tuple(r.results[0][f"out_{i}_dram"] for i in range(len(_OUTS)))
    return got[0]
```

```python
import concourse.bass as bass
from concourse import mybir
from contextlib import ExitStack


def recommender_kernel(nc, dense, indices, w0, b0, w1, b1, w2, b2, tables, wp, bp, out):
    fp32 = mybir.dt.float32
    i32 = mybir.dt.int32
    ALU = mybir.AluOpType
    ACT = mybir.ActivationFunctionType

    P = 128
    Q = 32
    BATCH, FEATURES = dense.shape
    TABLES, VOCAB, D = tables.shape
    H0, H1, OUT = w0.shape[1], w1.shape[1], wp.shape[1]
    TILES = BATCH // P
    SLOTS = 2
    STEPS = TILES // SLOTS
    N = TABLES + 1
    HALF = (N - 1) // 2
    ROWS = 9
    CHUNKS = N // ROWS
    PAIRS = ROWS * HALF
    assert N % 2 == 1 and N % ROWS == 0 and PAIRS < P and D == P and w2.shape[1] == D
    GROUP = 4
    GROUPS = -(-TABLES // GROUP)
    K0, K1 = H0 // P, H1 // P
    MLP_MM = K0 + K1 + 1
    assert GROUPS == MLP_MM
    MLP_EV = K0 + K1 + SLOTS
    MLP_LOADS = 5 + K1

    table_rows = tables.rearrange("t v d -> (t v) d")
    out_rows = out.rearrange("(p t) n -> t p n", t=TILES)

    def group_tables(k):
        return range(k * GROUP, min(TABLES, (k + 1) * GROUP))

    ctx = ExitStack()
    with ctx:
        def sb(name, shape, dt=fp32):
            return ctx.enter_context(nc.sbuf_tensor(name, shape, dt))

        def ps(name, shape):
            return ctx.enter_context(nc.psum_tensor(name, shape, fp32))

        def sem(name):
            return ctx.enter_context(nc.semaphore(name))

        def slot_sems(name):
            return [sem(f"{name}{s}") for s in range(SLOTS)]

        ident = sb("ident", [P, P])
        raw_idx = sb("raw_idx", [TABLES, P, TILES], i32)
        float_idx = sb("float_idx", [TABLES, TILES, P])
        table_i = sb("table_i", [P, TABLES], i32)
        table = sb("table", [P, TABLES])
        table_plus = sb("table_plus", [P, TILES, TABLES])
        row_idx = sb("row_idx", [P, TILES + SLOTS, TABLES], i32)
        idx = [sb(f"idx{s}", [P, TABLES], i32) for s in range(SLOTS)]
        dense_sb = sb("dense_sb", [P, TILES, FEATURES])
        denseT = sb("denseT", [FEATURES + 1, TILES * P])
        features = sb("features", [FEATURES + 1, SLOTS * P])
        w0_sb = sb("w0_sb", [FEATURES + 1, H0])
        w1_sb = sb("w1_sb", [P, K0, H1])
        w2_sb = sb("w2_sb", [P, K1, D])
        b1_sb = sb("b1_sb", [P, K1])
        b2_sb = sb("b2_sb", [P, 1])
        h0 = sb("h0", [P, K0, SLOTS * P])
        h1 = sb("h1", [P, K1, SLOTS * P])
        wp_mlp = sb("wp_mlp", [P, OUT])
        wp_pair = sb("wp_pair", [PAIRS + 1, CHUNKS, OUT])
        rows = [sb(f"rows{s}", [P, TABLES, D]) for s in range(SLOTS)]
        vecT = [sb(f"vecT{s}", [P, P, N]) for s in range(SLOTS)]
        prod = sb("prod", [P, N + HALF, Q])
        pairs = sb("pairs", [P, CHUNKS, PAIRS])
        pairT = sb("pairT", [P, CHUNKS, P])
        out_sb = [sb(f"out_sb{s}", [P, OUT]) for s in range(SLOTS)]

        trans_ps = [ps(f"trans_ps{k}", [P, GROUP, P]) for k in range(2)]
        gram_ps = ps("gram_ps", [P, 2, 512])
        pair_ps = ps("pair_ps", [P, CHUNKS + 1, P])
        out_ps = ps("out_ps", [P, OUT])
        mlp_ps = ps("mlp_ps", [P, 2, 512])

        idx_loaded = sem("idx_loaded")
        dense_loaded = sem("dense_loaded")
        mlp_loaded = sem("mlp_loaded")
        wp_loaded = sem("wp_loaded")
        ident_zeroed = sem("ident_zeroed")
        ident_ready = sem("ident_ready")
        table_i_ready = sem("table_i_ready")
        ones_ready = sem("ones_ready")
        gram_zeroed = sem("gram_zeroed")
        first_float = sem("first_float")
        other_float = sem("other_float")
        idx_turned = sem("idx_turned")
        idx_step = sem("idx_step")
        denseT_done = sem("denseT_done")
        denseT_copied = sem("denseT_copied")
        idx_ready = slot_sems("idx_ready")
        gather_begun = sem("gather_begun")
        gathered = [[sem(f"gathered{s}_{k}") for k in range(GROUPS)] for s in range(SLOTS)]
        transposed = sem("transposed")
        copied_dve = sem("copied_dve")
        copied_act = sem("copied_act")
        features_ready = sem("features_ready")
        mlp_done = sem("mlp_done")
        mlp_copied = sem("mlp_copied")
        gram_done = sem("gram_done")
        turned = sem("turned")
        wrapped = sem("wrapped")
        packed = sem("packed")
        pairs_done = sem("pairs_done")
        pairs_copied = sem("pairs_copied")
        projected = sem("projected")
        out_copied = sem("out_copied")
        out_sb_free = sem("out_sb_free")
        stored = slot_sems("stored")

        def wp_loads():
            def row(lo, hi):
                return D + lo * (N - 1) - lo * (lo - 1) // 2 + hi - lo - 1
            for r in range(N - 1):
                yield r // ROWS, HALF * (r % ROWS), 1, min(HALF, N - 1 - r), row(r, r + 1)
            for lo in range(N - HALF - 1):
                for c in range(CHUNKS):
                    first, last = max(lo + HALF + 1, ROWS * c), min(N, ROWS * (c + 1))
                    if first < last:
                        k = lo + N - first
                        yield c, HALF * (first - ROWS * c) + k - 1, HALF - 1, last - first, row(lo, first)

        WP_LOADS = list(wp_loads())
        assert sum(load[3] for load in WP_LOADS) == CHUNKS * PAIRS

        block = ctx.enter_context(nc.Block())

        @block.sync
        def _(sp):
            sp.dma_start(raw_idx[:, :, :], indices.rearrange("n (p t) -> n p t", t=TILES)).then_inc(idx_loaded, 16)
            sp.dma_start(wp_mlp[:, :], wp[0:D, :]).then_inc(wp_loaded, 16)
            sp.dma_start(wp_pair[PAIRS:PAIRS + 1, CHUNKS - 1, :], bp.rearrange("(a n) -> a n", a=1))\
                .then_inc(wp_loaded, 16)
            for chunk, part, step, count, first in WP_LOADS:
                sp.dma_start(wp_pair[part:part + step * (count - 1) + 1:step, chunk, :],
                             wp[first:first + count, :]).then_inc(wp_loaded, 16)
            with sp.Fori(0, STEPS) as i:
                for s in range(SLOTS):
                    sp.wait_ge(out_copied, SLOTS * i + s + 2)
                    sp.dma_start(out_rows[bass.ds(SLOTS * i + s, 1), :, :].rearrange("a p n -> (a p) n"),
                                 out_sb[s][:, :]).then_inc(stored[s], 16)
                    sp.wait_ge(stored[s], 16 * (i + 1))
                    sp.sem_inc(out_sb_free, 1)

        @block.gpsimd
        def _(pool):
            pool.memset(ident[:, :], 0.0).then_inc(ident_zeroed, 1)
            pool.iota(table_i[:, :], [[1, TABLES]], base=0, channel_multiplier=0).then_inc(table_i_ready, 1)
            pool.wait_ge(ident_zeroed, 1)
            pool.affine_select(out=ident[:, :], in_=ident[:, :], compare_op=ALU.not_equal, fill=1.0, base=0,
                               pattern=[[-1, P]], channel_multiplier=1).then_inc(ident_ready, 1)
            with pool.Fori(0, STEPS) as i:
                for s in range(SLOTS):
                    pool.wait_ge(idx_ready[s], i + 1)
                    pool.sem_inc(gather_begun, 1)
                    for n in range(TABLES):
                        pool.indirect_dma_start(
                            out=rows[s][:, n, :], out_offset=None, in_=table_rows,
                            in_offset=bass.IndirectOffsetOnAxis(ap=idx[s][:, n:n + 1], axis=0),
                        ).then_inc(gathered[s][n // GROUP], 16)

        @block.tensor
        def _(pe):
            pe.wait_ge(ident_ready, 1)
            pe.wait_ge(first_float, 1)
            pe.transpose(trans_ps[0][:, 0, 0:TABLES], float_idx[:, 0, :], ident[0:TABLES, 0:TABLES])\
                .then_inc(idx_turned, 1)
            pe.wait_ge(other_float, 1)
            for t in range(1, TILES):
                mm = pe.transpose(out_ps[:, t * TABLES:(t + 1) * TABLES], float_idx[:, t, :],
                                  ident[0:TABLES, 0:TABLES])
            mm.then_inc(idx_turned, 1)
            pe.wait_ge(dense_loaded, 16)
            for t in range(TILES):
                if t % 4 == 0 and t >= 8:
                    pe.wait_ge(denseT_copied, t // 4 - 1)
                mm = pe.matmul(mlp_ps[0:FEATURES, (t // 4) % 2, (t % 4) * P:(t % 4 + 1) * P],
                               dense_sb[:, t, :], ident[:, :], start=True, stop=True)
                if t % 4 == 3:
                    mm.then_inc(denseT_done, 1)
            pe.wait_ge(mlp_loaded, MLP_LOADS * 16)

            def mlp_block(i, c):
                pe.wait_ge(mlp_copied, MLP_EV * i + max(c, 1))
                dst = mlp_ps[:, c % 2, 0:SLOTS * P]
                if c < K0:
                    pe.wait_ge(features_ready, i + 1)
                    mm = pe.matmul(dst, w0_sb[:, c * P:(c + 1) * P], features[:, :], start=True, stop=True)
                elif c < K0 + K1:
                    pe.wait_ge(mlp_copied, MLP_EV * i + K0 + 1)
                    for k in range(K0):
                        mm = pe.matmul(dst, w1_sb[:, k, (c - K0) * P:(c - K0 + 1) * P], h0[:, k, :],
                                       start=(k == 0), stop=(k == K0 - 1))
                else:
                    pe.wait_ge(mlp_copied, MLP_EV * i + K0 + K1 + 1)
                    for k in range(K1):
                        mm = pe.matmul(dst, w2_sb[:, k, :], h1[:, k, :], start=(k == 0), stop=(k == K1 - 1))
                mm.then_inc(mlp_done, 1)

            with pe.Fori(0, STEPS) as i:
                pe.wait_ge(wp_loaded, 16 * (2 + len(WP_LOADS)))
                pe.wait_ge(ones_ready, 2)
                pe.wait_ge(gram_zeroed, 1)
                for s in range(SLOTS):
                    for k in range(GROUPS):
                        g = GROUPS * s + k
                        if s == 0:
                            mlp_block(i, k)
                        if k == GROUPS - 1:
                            pe.wait_ge((copied_dve, copied_act)[(g - 1) % 2], GROUPS * i + (g - 1) // 2 + 2)
                        pe.wait_ge(gathered[s][k], 16 * len(group_tables(k)) * (i + 1))
                        pe.wait_ge((copied_dve, copied_act)[g % 2], GROUPS * i + g // 2 + 1)
                        for n in group_tables(k):
                            mm = pe.transpose(trans_ps[g % 2][:, n % GROUP, :], rows[s][:, n, :], ident[:, :])
                        mm.then_inc(transposed, 1)
                    pe.wait_ge(mlp_copied, MLP_EV * i + K0 + K1 + s + 2)
                    pe.wait_ge((copied_dve, copied_act)[g % 2], GROUPS * i + g // 2 + 2)
                    for g in range(Q):
                        for j in range(P // Q):
                            v = vecT[s][:, Q * j + g, :]
                            mm = pe.matmul(gram_ps[Q * j:Q * j + N, g // 16, (g % 16) * N:(g % 16 + 1) * N],
                                           v, v, start=True, stop=True)
                    mm.then_inc(gram_done, 1)
                    pe.wait_ge(out_copied, SLOTS * i + s + 1)
                    pe.matmul(out_ps[:, :], vecT[s][:, :, 0], wp_mlp[:, :], start=True, stop=False)
                    pe.wait_ge(packed, SLOTS * i + s + 1)
                    for c in range(CHUNKS):
                        mm = pe.transpose(pair_ps[0:PAIRS, c, :], pairs[:, c, :], ident[:, :])
                    mm.then_inc(pairs_done, 1)
                    pe.wait_ge(pairs_copied, SLOTS * i + s + 2)
                    for c in range(CHUNKS):
                        k = PAIRS + (c == CHUNKS - 1)
                        mm = pe.matmul(out_ps[:, :], pairT[0:k, c, :], wp_pair[0:k, c, :],
                                       start=False, stop=(c == CHUNKS - 1))
                    mm.then_inc(projected, 1)

        @block.scalar
        def _(act):
            act.dma_start(dense_sb[:, :, :], dense.rearrange("(p t) f -> p t f", t=TILES)).then_inc(dense_loaded, 16)
            act.dma_start(w0_sb[0:FEATURES, :], w0).then_inc(mlp_loaded, 16)
            act.dma_start(w0_sb[FEATURES:FEATURES + 1, :], b0.rearrange("(a n) -> a n", a=1)).then_inc(mlp_loaded, 16)
            act.dma_start(w1_sb[:, :, :], w1.rearrange("(k p) n -> p k n", p=P)).then_inc(mlp_loaded, 16)
            act.dma_start(w2_sb[:, :, :], w2.rearrange("(k p) n -> p k n", p=P)).then_inc(mlp_loaded, 16)
            for k in range(K1):
                act.dma_start(b1_sb[:, k:k + 1], b1[k * P:(k + 1) * P].rearrange("(p a) -> p a", a=1))\
                    .then_inc(mlp_loaded, 16)
            act.dma_start(b2_sb[:, :], b2.rearrange("(p a) -> p a", a=1)).then_inc(mlp_loaded, 16)
            for first in (mlp_copied, copied_act, out_copied):
                act.sem_inc(first, 1)
            act.sem_inc(out_sb_free, SLOTS)
            act.wait_ge(idx_loaded, 16)
            act.activation(float_idx[:, 1:TILES, :], raw_idx[:, :, 1:TILES].rearrange("n p t -> n t p"), ACT.Copy)\
                .then_inc(other_float, 1)
            act.wait_ge(ones_ready, 1)
            for h in range(TILES // 4):
                act.wait_ge(denseT_done, h + 1)
                act.activation(denseT[0:FEATURES, h * 4 * P:(h + 1) * 4 * P], mlp_ps[0:FEATURES, h % 2, :],
                               ACT.Copy).then_inc(denseT_copied, 1)
            act.wait_ge(mlp_loaded, MLP_LOADS * 16)

            def mlp_copy(i, c):
                act.wait_ge(mlp_done, MLP_MM * i + c + 1)
                src = mlp_ps[:, c % 2, 0:SLOTS * P]
                if c < K0:
                    act.activation(h0[:, c, :], src, ACT.Relu).then_inc(mlp_copied, 1)
                elif c < K0 + K1:
                    k = c - K0
                    act.activation(h1[:, k, :], src, ACT.Relu, bias=b1_sb[:, k:k + 1]).then_inc(mlp_copied, 1)
                else:
                    for s in range(SLOTS):
                        act.activation(vecT[s][:, :, 0], src[:, s * P:(s + 1) * P], ACT.Identity,
                                       bias=b2_sb[:, 0:1]).then_inc(mlp_copied, 1)

            with act.Fori(0, STEPS) as i:
                act.wait_ge(denseT_copied, TILES // 4)
                act.activation(features[:, :], denseT[:, bass.ds(i * (SLOTS * P), SLOTS * P)], ACT.Copy)\
                    .then_inc(features_ready, 1)
                for s in range(SLOTS):
                    for k in range(GROUPS):
                        g = GROUPS * s + k
                        if s == 0:
                            mlp_copy(i, k)
                        if g % 2:
                            act.wait_ge(transposed, SLOTS * GROUPS * i + g + 1)
                            m = len(group_tables(k))
                            act.activation(vecT[s][:, :, 1 + GROUP * k:1 + GROUP * k + m].rearrange("d b n -> d n b"),
                                           trans_ps[1][:, 0:m, :], ACT.Copy).then_inc(copied_act, 1)
                    act.wait_ge(turned, SLOTS * i + s + 2)
                    act.activation(prod[:, N:N + HALF, N - HALF:N], prod[:, 0:HALF, N - HALF:N], ACT.Copy)\
                        .then_inc(wrapped, 1)
                    act.wait_ge(wrapped, SLOTS * i + s + 1)
                    first = prod[:, 1, 0:1]
                    src = bass.AP(tensor=first.tensor, offset=first.offset,
                                  ap=[list(first.ap[0]), [Q + 1, N], [Q, HALF]])
                    act.activation(pairs[:, :, :].rearrange("p c (r k) -> p (c r) k", k=HALF), src, ACT.Copy)\
                        .then_inc(packed, 1)
                    act.wait_ge(projected, SLOTS * i + s + 1)
                    act.wait_ge(out_sb_free, SLOTS * i + s + 1)
                    act.activation(out_sb[s][:, :], out_ps[:, :], ACT.Copy).then_inc(out_copied, 1)

        @block.vector
        def _(dve):
            for first in (copied_dve, turned, pairs_copied):
                dve.sem_inc(first, 1)
            dve.wait_ge(table_i_ready, 1)
            dve.tensor_copy(table[:, :], table_i[:, :]).then_inc(idx_step, 1)
            dve.wait_ge(idx_loaded, 16)
            dve.tensor_copy(float_idx[:, 0, :], raw_idx[:, :, 0]).then_inc(first_float, 1)
            dve.memset(row_idx[:, TILES:TILES + SLOTS, :], 0).then_inc(idx_step, 1)

            def row_numbers(dst, src, first, last, steps):
                dve.tensor_scalar(src, src, float(VOCAB - 1), float(-VOCAB), ALU.min, ALU.max).then_inc(idx_step, 1)
                dve.wait_ge(idx_step, steps + 1)
                plus = table_plus[:, first:last, :]
                dve.scalar_tensor_tensor(out=plus, in0=src, scalar=0.0,
                                         in1=table[:, :].unsqueeze(1).to_broadcast([P, last - first, TABLES]),
                                         op0=ALU.is_lt, op1=ALU.add).then_inc(idx_step, 1)
                dve.wait_ge(idx_step, steps + 2)
                return dve.scalar_tensor_tensor(out=dst, in0=plus, scalar=float(VOCAB), in1=src,
                                                op0=ALU.mult, op1=ALU.add)

            dve.wait_ge(idx_turned, 1)
            row_numbers(idx[0][:, :].unsqueeze(1), trans_ps[0][:, 0:1, 0:TABLES], 0, 1, 2).then_inc(idx_ready[0], 1)
            dve.memset(denseT[:, :], 1.0).then_inc(ones_ready, 1)
            dve.wait_ge(idx_turned, 2)
            row_numbers(row_idx[:, 1:TILES, :], out_ps[:, TABLES:TILES * TABLES].rearrange("p (t n) -> p t n", n=TABLES),
                        1, TILES, 4).then_inc(idx_step, 1)
            dve.wait_ge(idx_step, 7)
            for s in range(1, SLOTS):
                dve.tensor_copy(idx[s][:, :], row_idx[:, s, :]).then_inc(idx_ready[s], 1)
            dve.memset(pairT[:, :, :], 1.0).then_inc(ones_ready, 1)
            dve.memset(gram_ps[:, :, :], 0.0).then_inc(gram_zeroed, 1)
            with dve.Fori(0, STEPS) as i:
                for s in range(SLOTS):
                    for k in range(GROUPS):
                        g = GROUPS * s + k
                        if g % 2 == 0:
                            dve.wait_ge(transposed, SLOTS * GROUPS * i + g + 1)
                            m = len(group_tables(k))
                            dve.tensor_copy(vecT[s][:, :, 1 + GROUP * k:1 + GROUP * k + m].rearrange("d b n -> d n b"),
                                            trans_ps[0][:, 0:m, :]).then_inc(copied_dve, 1)
                    dve.wait_ge(transposed, SLOTS * GROUPS * i + GROUPS * (s + 1))
                    dve.tensor_copy(idx[s][:, :],
                                    row_idx[:, bass.ds(SLOTS * i + SLOTS + s, 1), :].rearrange("p a n -> p (a n)"))\
                        .then_inc(idx_ready[s], 1)
                    dve.wait_ge(gram_done, SLOTS * i + s + 1)
                    src = bass.AP(tensor=gram_ps[:, :, :].tensor, offset=gram_ps[:, :, :].offset,
                                  ap=[list(gram_ps[:, :, :].ap[0]), [1, N], [512, 2], [N, 16]])
                    dve.transpose(prod[:, 0:N, :], src).then_inc(turned, 1)
                    dve.wait_ge(pairs_done, SLOTS * i + s + 1)
                    dve.tensor_copy(pairT[0:PAIRS, :, :], pair_ps[0:PAIRS, 0:CHUNKS, :]).then_inc(pairs_copied, 1)


_INS = ['r_dense', 'r_emb_indices', 'L0_rec_W0', 'L0_rec_b0', 'L0_rec_W1', 'L0_rec_b1', 'L0_rec_W2',
        'L0_rec_b2', 'L0_rec_emb_tables', 'L0_rec_Wp', 'L0_rec_bp']
_OUTS = [((2048, 512), 'float32')]


def kernel(**inputs):
    import numpy as _np
    import concourse.bacc as _bacc
    from concourse import mybir as _mybir
    from concourse.bass_utils import run_bass_kernel_spmd as _run

    nc = _bacc.Bacc("TRN2", target_bir_lowering=False, num_devices=1)
    arrays, args = {}, []
    for name in _INS:
        a = _np.ascontiguousarray(inputs[name])
        arrays[f"in_{name}_dram"] = a
        args.append(nc.dram_tensor(f"in_{name}_dram", a.shape, _mybir.dt.from_np(a.dtype), kind="ExternalInput").ap())
    for i, (shape, dtype) in enumerate(_OUTS):
        dt = _mybir.dt.from_np(_np.dtype(dtype))
        args.append(nc.dram_tensor(f"out_{i}_dram", shape, dt, kind="ExternalOutput").ap())
    recommender_kernel(nc, *args)
    r = _run(nc, [arrays], core_ids=[0])
    got = tuple(r.results[0][f"out_{i}_dram"] for i in range(len(_OUTS)))
    return got[0]
```
